# Optimizing a Trainium2 kernel written in Bass

```python
import numpy as np
import jax
import jax.numpy as jnp

def _softmax(x, axis=-1):
    return jax.nn.softmax(x, axis=axis)
def _gelu(x):
    return jax.nn.gelu(x, approximate=True)
def _silu(x):
    return jax.nn.silu(x)
def _sigmoid(x):
    return jax.nn.sigmoid(x)
def _layernorm(x, axis=-1, eps=1e-5):
    m = jnp.mean(x, axis=axis, keepdims=True)
    v = jnp.var(x, axis=axis, keepdims=True)
    return (x - m) / jnp.sqrt(v + eps)
def _scatter_add(tgt, idx, src, axis=0):
    return tgt.at[idx].add(src)
def _segment_sum(src, seg, n):
    return jax.ops.segment_sum(src, seg, n)

kernel_name = 'mk_conv_seq_d1_conv_nchw32_8a6eb4'

def setup_inputs(seed: int = 0):
    np.random.seed(seed)
    _w = jnp.asarray
    def _rec_inputs():
        import jax
        import jax.numpy as jnp
        _gk = jax.random.key(seed)
        x = -7.109e-05 + 0.9999 * jax.random.normal(jax.random.fold_in(_gk, 1), (8, 32, 512, 512), jnp.float32)
        return x
    x = _rec_inputs()
    def _L0_conv_setup():
        import jax, jax.numpy as jnp
        import numpy as np
        from jax import lax
        _H = np.array([0.11154074335008017, 0.4946238903983854, 0.7511339080215775, 0.3152503517092432, -0.22626469396516913, -0.12976686756709563, 0.09750160558707936, 0.02752286553001629, -0.031582039318031156, 0.0005538422009938016, 0.004777257511010651, -0.00107730108499558])
        _L = 12
        _RLO = _H
        _RHI = _H[::-1].copy()
        _RHI[1::2] *= -1.0
        _ANA = np.stack([_RLO, _RHI])
        _SYN = np.stack([_RLO[::-1], _RHI[::-1]])
        _LEVEL = 4

        def _afb1d(x, axis):
            x = jnp.moveaxis(x, axis, -1)
            N = x.shape[-1]
            out = (N + _L - 1) // 2
            p = 2 * (out - 1) - N + _L
            pad = [(0, 0)] * (x.ndim - 1) + [(p // 2, (p + 1) // 2)]
            xp = jnp.pad(x, pad, mode='symmetric')
            lead = xp.shape[:-1]
            xf = xp.reshape(-1, 1, xp.shape[-1])
            k = jnp.asarray(_ANA, x.dtype)[:, None, :]
            y = lax.conv_general_dilated(xf, k, (2,), 'VALID', dimension_numbers=('NCH', 'OIH', 'NCH'))
            y = y.reshape(*lead, 2, out)
            lo = jnp.moveaxis(y[..., 0, :], -1, axis)
            hi = jnp.moveaxis(y[..., 1, :], -1, axis)
            return (lo, hi)

        def _sfb1d(lo, hi, axis):
            lo = jnp.moveaxis(lo, axis, -1)
            hi = jnp.moveaxis(hi, axis, -1)
            lead = lo.shape[:-1]
            N = lo.shape[-1]
            xf = jnp.stack([lo.reshape(-1, N), hi.reshape(-1, N)], axis=1)
            k = jnp.asarray(_SYN, lo.dtype)[None, :, :]
            y = lax.conv_general_dilated(xf, k, (1,), [(1, 1)], lhs_dilation=(2,), dimension_numbers=('NCH', 'OIH', 'NCH'))
            y = y[:, 0].reshape(*lead, 2 * N + 2 - _L)
            return jnp.moveaxis(y, -1, axis)

        def _dwt2(x, J):
            ll, yh = (x, [])
            for _ in range(J):
                lo, hi = _afb1d(ll, -1)
                ll, lh = _afb1d(lo, -2)
                hl, hh = _afb1d(hi, -2)
                yh.append(jnp.stack([lh, hl, hh], axis=2))
            return (ll, yh)

        def _idwt2(yl, yh):
            ll = yl
            for h in yh[::-1]:
                if ll.shape[-2] > h.shape[-2]:
                    ll = ll[..., :-1, :]
                if ll.shape[-1] > h.shape[-1]:
                    ll = ll[..., :-1]
                lo = _sfb1d(ll, h[:, :, 0], -2)
                hi = _sfb1d(h[:, :, 1], h[:, :, 2], -2)
                ll = _sfb1d(lo, hi, -1)
            return ll
        key = jax.random.key(seed)
        k0, k1, k2 = jax.random.split(key, 3)
        B, CIN, COUT, HW = (8, 32, 32, 512)
        HC = 42
        scale = 1.0 / (CIN * COUT)
        x = jax.random.normal(k0, (B, CIN, HW, HW), dtype=jnp.float32)
        w_yl = scale * jax.random.uniform(k1, (CIN, COUT, HC, HC), dtype=jnp.float32)
        w_yh = scale * jax.random.uniform(k2, (CIN, COUT, 3, HC, HC), dtype=jnp.float32)
        return {'x': x, 'w_yl': w_yl, 'w_yh': w_yh}
    _L0_conv_all = _L0_conv_setup()
    _L0_conv_in = {k: v for k, v in _L0_conv_all.items() if k in ('w_yl', 'w_yh', )}
    del _L0_conv_all

    return {
        "x": x,
        "L0_conv_w_yl": _L0_conv_in["w_yl"],
        "L0_conv_w_yh": _L0_conv_in["w_yh"],
    }

def reference(x, L0_conv_w_yl, L0_conv_w_yh):
    import jax
    import jax.numpy as jnp
    def _L0_conv_ref(x, w_yl, w_yh):
        import jax, jax.numpy as jnp
        import numpy as np
        from jax import lax
        _H = np.array([0.11154074335008017, 0.4946238903983854, 0.7511339080215775, 0.3152503517092432, -0.22626469396516913, -0.12976686756709563, 0.09750160558707936, 0.02752286553001629, -0.031582039318031156, 0.0005538422009938016, 0.004777257511010651, -0.00107730108499558])
        _L = 12
        _RLO = _H
        _RHI = _H[::-1].copy()
        _RHI[1::2] *= -1.0
        _ANA = np.stack([_RLO, _RHI])
        _SYN = np.stack([_RLO[::-1], _RHI[::-1]])
        _LEVEL = 4

        def _afb1d(x, axis):
            x = jnp.moveaxis(x, axis, -1)
            N = x.shape[-1]
            out = (N + _L - 1) // 2
            p = 2 * (out - 1) - N + _L
            pad = [(0, 0)] * (x.ndim - 1) + [(p // 2, (p + 1) // 2)]
            xp = jnp.pad(x, pad, mode='symmetric')
            lead = xp.shape[:-1]
            xf = xp.reshape(-1, 1, xp.shape[-1])
            k = jnp.asarray(_ANA, x.dtype)[:, None, :]
            y = lax.conv_general_dilated(xf, k, (2,), 'VALID', dimension_numbers=('NCH', 'OIH', 'NCH'))
            y = y.reshape(*lead, 2, out)
            lo = jnp.moveaxis(y[..., 0, :], -1, axis)
            hi = jnp.moveaxis(y[..., 1, :], -1, axis)
            return (lo, hi)

        def _sfb1d(lo, hi, axis):
            lo = jnp.moveaxis(lo, axis, -1)
            hi = jnp.moveaxis(hi, axis, -1)
            lead = lo.shape[:-1]
            N = lo.shape[-1]
            xf = jnp.stack([lo.reshape(-1, N), hi.reshape(-1, N)], axis=1)
            k = jnp.asarray(_SYN, lo.dtype)[None, :, :]
            y = lax.conv_general_dilated(xf, k, (1,), [(1, 1)], lhs_dilation=(2,), dimension_numbers=('NCH', 'OIH', 'NCH'))
            y = y[:, 0].reshape(*lead, 2 * N + 2 - _L)
            return jnp.moveaxis(y, -1, axis)

        def _dwt2(x, J):
            ll, yh = (x, [])
            for _ in range(J):
                lo, hi = _afb1d(ll, -1)
                ll, lh = _afb1d(lo, -2)
                hl, hh = _afb1d(hi, -2)
                yh.append(jnp.stack([lh, hl, hh], axis=2))
            return (ll, yh)

        def _idwt2(yl, yh):
            ll = yl
            for h in yh[::-1]:
                if ll.shape[-2] > h.shape[-2]:
                    ll = ll[..., :-1, :]
                if ll.shape[-1] > h.shape[-1]:
                    ll = ll[..., :-1]
                lo = _sfb1d(ll, h[:, :, 0], -2)
                hi = _sfb1d(h[:, :, 1], h[:, :, 2], -2)
                ll = _sfb1d(lo, hi, -1)
            return ll
        yl, yh = _dwt2(x, _LEVEL)
        yl_out = jnp.einsum('bixy,ioxy->boxy', yl, w_yl)
        yh_out = yh[:-1] + [jnp.einsum('bicxy,iocxy->bocxy', yh[-1], w_yh)]
        return _idwt2(yl_out, yh_out)

    def _gn(v, G=16, eps=1e-5):
        B_, C_, H_, W_ = v.shape
        g = v.reshape(B_, G, C_ // G, H_, W_)
        m = jnp.mean(g, axis=(2, 3, 4), keepdims=True)
        s = jnp.var(g, axis=(2, 3, 4), keepdims=True)
        return ((g - m) / jnp.sqrt(s + eps)).reshape(v.shape)

    def _ln_c(v, eps=1e-6):
        m = jnp.mean(v, axis=1, keepdims=True)
        s = jnp.var(v, axis=1, keepdims=True)
        return (v - m) / jnp.sqrt(s + eps)

    def _ln_t(v, eps=1e-5):
        m = jnp.mean(v, axis=-1, keepdims=True)
        s = jnp.var(v, axis=-1, keepdims=True)
        return (v - m) / jnp.sqrt(s + eps)

    def _to_tokens(v):
        B_, C_, H_, W_ = v.shape
        return v.reshape(B_, C_, H_ * W_).transpose(0, 2, 1)
    def _from_tokens(t, like):
        B_, C_, H_, W_ = like.shape
        return t.transpose(0, 2, 1).reshape(B_, C_, H_, W_)

    x = _L0_conv_ref(x, L0_conv_w_yl, L0_conv_w_yh)
    return x


_drawn_inputs = setup_inputs


def setup_inputs(seed=0):
    import zlib

    import numpy as np

    out = dict(_drawn_inputs(seed))
    spreads = {}
    factors = {'L0_conv_w_yl': 200.0, 'L0_conv_w_yh': 200.0}
    for name, (base, spread) in spreads.items():
        noise = np.random.default_rng([zlib.crc32(name.encode()), seed]).standard_normal(out[name].shape)
        drawn = base * np.exp(spread * noise) if base else spread * noise
        out[name] = jnp.asarray(drawn.astype(out[name].dtype))
    for name, factor in factors.items():
        out[name] = (out[name] * factor).astype(out[name].dtype)
    return out
```

```python
from contextlib import ExitStack

import numpy as np
import concourse.bass as bass
from concourse import mybir
from concourse.alu_op_type import AluOpType as ALU

F32 = mybir.dt.float32

P = 128
BATCH, CHANNELS, SIZE = 8, 32, 512
IMAGES = BATCH * CHANNELS
CHUNKS = SIZE // P
BANDS, COEFS = 2, 42
ROWS = BANDS * COEFS
HALF = COEFS // 2
HALF_ROWS = BANDS * HALF
WIN = 26
SHIFT = COEFS - WIN
BOTH = WIN - SHIFT

SLOTS = 4
GROUP = 4
BODY = 8
TURNS = IMAGES // BODY

PLACES = ROWS * ROWS // 4
TILES = 4
PLACES_TILE = PLACES // TILES
U = 7
MIX_CHUNKS = PLACES_TILE // U
MIX_BUFS = 3
MIX_TURNS = MIX_CHUNKS // MIX_BUFS
QB = 4 * BATCH

LO = np.array([0.11154074335008017, 0.4946238903983854, 0.7511339080215775, 0.3152503517092432,
               -0.22626469396516913, -0.12976686756709563, 0.09750160558707936, 0.02752286553001629,
               -0.031582039318031156, 0.0005538422009938016, 0.004777257511010651, -0.00107730108499558])
TAPS = len(LO)
HI = LO[::-1] * np.where(np.arange(TAPS) % 2, -1.0, 1.0)
LEVELS = 4


def analysis(n, taps):
    out = (n + TAPS - 1) // 2
    pad = (2 * (out - 1) - n + TAPS) // 2
    m = np.zeros((out, n))
    for r in range(out):
        for k in range(TAPS):
            c = 2 * r + k - pad
            c = -1 - c if c < 0 else c
            c = 2 * n - 1 - c if c >= n else c
            m[r, c] += taps[k]
    return m


def synthesis(n, taps):
    m = np.zeros((2 * n + 2 - TAPS, n))
    for s in range(m.shape[0]):
        for r in range(n):
            k = s + TAPS - 2 - 2 * r
            if 0 <= k < TAPS:
                m[s, r] = taps[k]
    return m


def transforms():
    a, s, sizes = np.eye(SIZE), np.eye(SIZE), [SIZE]
    for _ in range(LEVELS - 1):
        a = analysis(sizes[-1], LO) @ a
        s = s @ synthesis(a.shape[0], LO)[:sizes[-1]]
        sizes.append(a.shape[0])
    n = sizes[-1]
    return (np.stack([analysis(n, t) @ a for t in (LO, HI)]),
            np.stack([s @ synthesis(COEFS, t)[:n] for t in (LO, HI)], axis=1))


AH, AW, SW, SH, EYE, NEG = 0, 256, 640, 1152, 1664, 1792
CONSTS = NEG + 32


def constants():
    a, s = transforms()
    c = np.zeros((P, CONSTS))
    for k in range(CHUNKS):
        rows = slice(k * P, (k + 1) * P)
        first = SHIFT * (k // 2)
        c[:, AH + 64 * k:AH + 64 * k + BANDS * WIN] = a[:, first:first + WIN, rows].reshape(BANDS * WIN, P).T
    for j in range(2):
        for n in range(3):
            rows = slice((j + n) * P, (j + n + 1) * P)
            at = AW + 64 * (3 * j + n)
            c[:, at:at + HALF_ROWS] = a[:, HALF * j:HALF * (j + 1), rows].reshape(HALF_ROWS, P).T
    c[:ROWS, SW:SW + SIZE] = s.reshape(SIZE, BANDS, 2, HALF).transpose(2, 1, 3, 0).reshape(ROWS, SIZE)
    c[:ROWS, SH:SH + SIZE] = s.reshape(SIZE, ROWS).T
    c[:, EYE:EYE + P] = np.eye(P)
    c[:, NEG:NEG + 32] = -np.tile(np.eye(32), (4, 1))
    return c.astype(np.float32)


def wavelet_mix_kernel(nc, x, weights, consts, out):
    coef_dram = nc.dram_tensor("coef_dram", (IMAGES, ROWS, ROWS), F32, kind="Internal").ap()
    delta_dram = nc.dram_tensor("delta_dram", (IMAGES, ROWS, ROWS), F32, kind="Internal").ap()
    x_rows = x.rearrange("b i (c p) w -> (b i) p c w", p=P)
    out_rows = out.rearrange("b i (c p) w -> (b i) p c w", p=P)

    with ExitStack() as ctx:
        def sb(name, shape):
            return ctx.enter_context(nc.sbuf_tensor(name, shape, F32))

        def sem(name):
            return ctx.enter_context(nc.semaphore(name))

        def sems(name, n):
            return [sem(f"{name}{i}") for i in range(n)]

        const = sb("const", [P, CONSTS])
        x_sb = sb("x_sb", [P, SLOTS, CHUNKS, SIZE])
        along_h = sb("along_h", [P, 2, SIZE])
        turned = sb("turned", [P, 2, CHUNKS, GROUP, ROWS])
        coef_sb = sb("coef_sb", [P, 2, GROUP, ROWS])
        delta_sb = sb("delta_sb", [P, 2, GROUP, P])
        spread = sb("spread", [P, 2, SIZE])
        mix_in = sb("mix_in", [P, BATCH, PLACES])
        mix_out = sb("mix_out", [P, BATCH, 4, PLACES_TILE])
        w_sb = sb("w_sb", [P, MIX_BUFS, U, TILES, CHANNELS])
        diag = sb("diag", [P, MIX_BUFS, TILES, U, QB])

        ps = ctx.enter_context(nc.psum_tensor("ps", [P, 8, 512], F32))

        const_loaded = sem("const_loaded")
        cleared = sem("cleared")
        x_loaded = sems("x_loaded", SLOTS)
        h_done = sems("h_done", SLOTS)
        h_copied = sems("h_copied", 2)
        t_done = sems("t_done", 2)
        t_copied = sems("t_copied", 2)
        t_half = sems("t_half", 2)
        w_done = sems("w_done", 2)
        c_copied = sems("c_copied", 2)
        c_stored = sems("c_stored", 2)
        mix_in_loaded = sem("mix_in_loaded")
        w_loaded = sems("w_loaded", MIX_BUFS)
        diag_built = sems("diag_built", MIX_BUFS)
        mixed = sems("mixed", MIX_BUFS)
        mixed_copied = sems("mixed_copied", MIX_BUFS)
        d_stored = sem("d_stored")
        d_loaded = sems("d_loaded", 2)
        s_done = sems("s_done", 2)
        s_copied = sems("s_copied", 2)
        o_done = sems("o_done", 2)
        added = sems("added", 2)
        x_stored = sems("x_stored", SLOTS)

        ctx.enter_context(nc.allow_non_contiguous_dma(reason="rows of 84 coefficients"))
        block = ctx.enter_context(nc.Block())

        @block.sync
        def _(sp):
            sp.dma_start(const[:], consts).then_inc(const_loaded, 16)

            def load_x(c, g, before):
                slot, use = c % SLOTS, 2 * g + c // SLOTS + before
                sp.dma_start(x_sb[:, slot], x_rows[BODY * g + c]).then_inc(x_loaded[slot], 16)

            for c in range(SLOTS):
                load_x(c, 0, 0)
            for c in range(SLOTS, BODY):
                sp.wait_ge(h_done[c % SLOTS], 1)
                load_x(c, 0, 0)
            with sp.Fori(1, TURNS) as g:
                for c in range(BODY):
                    sp.wait_ge(h_done[c % SLOTS], 2 * g + c // SLOTS)
                    load_x(c, g, 0)

            for c in range(SLOTS):
                sp.wait_ge(h_done[c], 2 * TURNS)
                load_x(c, 0, 2 * TURNS)

            for b in range(MIX_BUFS):
                sp.dma_start(w_sb[:, b], weights[b]).then_inc(w_loaded[b], 16)
            for p in range(2):
                sp.wait_ge(c_stored[p], 32 * TURNS)
            coef_q = coef_dram.rearrange("(b i) (q r) h -> q i b (r h)", b=BATCH, q=4)
            for q in range(4):
                sp.dma_start(mix_in[32 * q:32 * q + 32], coef_q[q]).then_inc(mix_in_loaded, 16)
            with sp.Fori(1, MIX_TURNS) as t:
                for b in range(MIX_BUFS):
                    sp.wait_ge(mixed[b], t)
                    sp.dma_start(w_sb[:, b], weights[MIX_BUFS * t + b]).then_inc(w_loaded[b], 16)
            for b in range(MIX_BUFS):
                sp.wait_ge(mixed_copied[b], MIX_TURNS)
            delta_q = delta_dram.rearrange("(b o) (q r) h -> o b q (r h)", b=BATCH, q=4)
            for tile in range(TILES):
                for b in range(BATCH):
                    sp.dma_start(delta_q[:, b, :, tile * PLACES_TILE:(tile + 1) * PLACES_TILE],
                                 mix_out[32 * tile:32 * tile + 32, b]).then_inc(d_stored, 16)
            sp.wait_ge(d_stored, 16 * TILES * BATCH)

            delta_g = delta_dram.rearrange("(n g) w h -> n w g h", g=GROUP)

            def load_delta(n, buf):
                sp.dma_start(delta_sb[0:ROWS, buf, :, 0:ROWS], delta_g[n]).then_inc(d_loaded[buf], 16)

            def store(c, g):
                slot = c % SLOTS
                sp.wait_ge(added[1], BODY * g + c + 1)
                sp.dma_start(out_rows[BODY * g + c], x_sb[:, slot]).then_inc(x_stored[slot], 16)

            def next_x(c, g):
                slot = (c - 1) % SLOTS
                sp.wait_ge(x_stored[slot], 16 * (2 * g + (c - 1) // SLOTS + 1))
                load_x(c + 3, g, 2 * TURNS)

            sp.wait_ge(cleared, 1)
            load_delta(0, 0)
            load_delta(1, 1)
            store(0, 0)
            def turn(g):
                for c in range(1, BODY + 1):
                    store(c, g)
                    next_x(c, g)
                    if c == GROUP - 1:
                        load_delta(2 * g + 2, 0)
                    if c == BODY - 1:
                        load_delta(2 * g + 3, 1)
            turn(0)
            with sp.Fori(1, TURNS - 1) as g:
                turn(g)
            for c in range(1, BODY):
                store(c, TURNS - 1)
                if c + 3 < BODY:
                    next_x(c, TURNS - 1)
            for s in range(SLOTS):
                sp.wait_ge(x_stored[s], 16 * 2 * TURNS)

        @block.tensor
        def _(pe):
            pe.wait_ge(const_loaded, 16)

            def h_stage(c, g):
                slot, use, p = c % SLOTS, 2 * g + c // SLOTS, c % 2
                pe.wait_ge(x_loaded[slot], 16 * (use + 1))
                pe.wait_ge(h_copied[p], BODY // 2 * g + c // 2)
                for k in (0, 2, 1, 3):
                    j = k // 2
                    last = nc.tensor.matmul(ps[64 * j:64 * j + 64, p], const[:, AH + 64 * k:AH + 64 * k + 64],
                                            x_sb[:, slot, k], start=k % 2 == 0, stop=k % 2 == 1)
                last.then_inc(h_done[slot], 1)

            def turn_stage(c, g):
                p, n = c % 2, BODY // 2 * g + c // 2
                pe.wait_ge(h_copied[p], n + 1)
                pe.wait_ge(t_copied[p], n)
                for k in range(CHUNKS):
                    last = nc.tensor.matmul(ps[:, 2 + p, P * k:P * k + P], along_h[:, p, P * k:P * k + P],
                                            const[:, EYE:EYE + P], start=True, stop=True, is_transpose=True)
                last.then_inc(t_done[p], 1)

            def w_stage(buf, n):
                pe.wait_ge(t_copied[1], 2 * (2 * n + buf) + 2)
                pe.wait_ge(c_copied[buf], n)
                for k in range(3):
                    for j in range(2):
                        at = AW + 64 * (3 * j + k)
                        last = nc.tensor.matmul(ps[64 * j:64 * j + 64, 4 + buf, 0:GROUP * ROWS],
                                                const[:, at:at + 64],
                                                turned[:, buf, j + k].rearrange("p g r -> p (g r)"),
                                                start=k == 0, stop=k == 2)
                last.then_inc(w_done[buf], 1)

            def step(c, g):
                h_stage(c, g)
                if c:
                    turn_stage(c - 1, g)
                if c % GROUP == 1 and c > GROUP:
                    m = c // GROUP - 1
                    w_stage(m % 2, g + m // 2)

            for c in range(6):
                step(c, 0)
            def turn(g):
                for c in range(6, BODY + 6):
                    step(c, g)
            turn(0)
            with pe.Fori(1, TURNS - 1) as g:
                turn(g)
            for c in range(6, BODY):
                step(c, TURNS - 1)
            turn_stage(BODY - 1, TURNS - 1)
            w_stage(1, TURNS - 1)

            def mix(b, t):
                pe.wait_ge(diag_built[b], t + 1)
                pe.wait_ge(w_loaded[b], 16 * (t + 1))
                pe.wait_ge(mixed_copied[b], t)
                for tile in range(TILES):
                    nc.tensor.matmul(ps[32 * tile:32 * tile + 32, b, 0:U * QB], const[:, NEG:NEG + 32],
                                     diag[:, b, tile].rearrange("p u n -> p (u n)"), start=True, stop=False,
                                     skip_group_check=True)
                for u in range(U):
                    for tile in range(TILES):
                        last = nc.tensor.matmul(ps[32 * tile:32 * tile + 32, b, QB * u:QB * u + QB],
                                                w_sb[:, b, u, tile], diag[:, b, tile, u],
                                                start=False, stop=u == U - 1, skip_group_check=True)
                last.then_inc(mixed[b], 1)

            for p in range(2):
                pe.wait_ge(h_copied[p], IMAGES // 2)
                pe.wait_ge(t_copied[p], IMAGES // 2)
            def turn(t):
                for b in range(MIX_BUFS):
                    mix(b, t)
            turn(0)
            with pe.Fori(1, MIX_TURNS) as t:
                turn(t)
            for b in range(MIX_BUFS):
                pe.wait_ge(mixed_copied[b], MIX_TURNS)
            for p in range(2):
                pe.wait_ge(c_copied[p], TURNS)

            def spread_stage(c, g):
                p, buf = c % 2, c // GROUP % 2
                pe.wait_ge(d_loaded[buf], 16 * (g + c // BODY + 1))
                pe.wait_ge(s_copied[p], BODY // 2 * g + c // 2)
                nc.tensor.matmul(ps[:, p], delta_sb[:, buf, c % GROUP], const[:, SW:SW + SIZE],
                                 start=True, stop=True).then_inc(s_done[p], 1)

            def out_stage(c, g):
                p, n = c % 2, BODY * g + c
                pe.wait_ge(s_copied[p], BODY // 2 * g + c // 2 + 1)
                for half in range(2):
                    pe.wait_ge(added[half], n)
                    for k in (2 * half, 2 * half + 1):
                        last = nc.tensor.matmul(ps[:, 2 + k], const[:, SH + P * k:SH + P * k + P], spread[:, p],
                                                start=True, stop=True)
                    last.then_inc(o_done[half], 1)

            spread_stage(0, 0)
            def turn(g):
                for c in range(BODY):
                    spread_stage(c + 1, g)
                    out_stage(c, g)
            turn(0)
            with pe.Fori(1, TURNS - 1) as g:
                turn(g)
            for c in range(BODY):
                if c < BODY - 1:
                    spread_stage(c + 1, TURNS - 1)
                out_stage(c, TURNS - 1)

        @block.scalar
        def _(act):
            def copy_h(c, g):
                p, n = c % 2, BODY // 2 * g + c // 2
                act.wait_ge(h_done[c % SLOTS], 2 * g + c // SLOTS + 1)
                act.wait_ge(t_done[p], n)
                nc.scalar.copy(along_h[:, p], ps[:, p]).then_inc(h_copied[p], 1)

            def copy_c(m, g):
                buf, n = m % 2, g + m // 2
                act.wait_ge(w_done[buf], n + 1)
                act.wait_ge(c_stored[buf], 32 * n)
                nc.scalar.copy(coef_sb[:, buf], ps[:, 4 + buf, 0:GROUP * ROWS]).then_inc(c_copied[buf], 1)
                act.wait_ge(c_copied[buf], n + 1)
                for j in range(2):
                    rows = coef_g[2 * g + m, HALF_ROWS * j:HALF_ROWS * (j + 1)]
                    act.dma_start(rows, coef_sb[64 * j:64 * j + HALF_ROWS, buf]).then_inc(c_stored[buf], 16)

            coef_g = coef_dram.rearrange("(n g) w h -> n w g h", g=GROUP)

            def step(c, g):
                copy_h(c, g)
                if c % GROUP == 2 and c > GROUP:
                    copy_c(c // GROUP - 1, g)

            for c in range(6):
                step(c, 0)
            def turn(g):
                for c in range(6, BODY + 6):
                    step(c, g)
            turn(0)
            with act.Fori(1, TURNS - 1) as g:
                turn(g)
            for c in range(6, BODY):
                step(c, TURNS - 1)
            copy_c(1, TURNS - 1)

            def turn(t):
                for b in range(MIX_BUFS):
                    act.wait_ge(mixed[b], t + 1)
                    nc.scalar.copy(mix_out[:, :, :, bass.ds(U * MIX_BUFS * t + U * b, U)],
                                   ps[:, b, 0:U * QB].rearrange("p (u q b) -> p b q u", q=4, b=BATCH),
                                   ).then_inc(mixed_copied[b], 1)
            turn(0)
            with act.Fori(1, MIX_TURNS) as t:
                turn(t)

            def turn(g):
                for c in range(BODY):
                    p, n = c % 2, BODY // 2 * g + c // 2
                    act.wait_ge(s_done[p], n + 1)
                    act.wait_ge(o_done[1], BODY * g + max(c - 1, 0))
                    nc.scalar.copy(spread[:, p], ps[:, p]).then_inc(s_copied[p], 1)
            turn(0)
            with act.Fori(1, TURNS) as g:
                turn(g)

        @block.vector
        def _(dve):
            nc.vector.memset(diag[:], 0.0)
            nc.vector.memset(delta_sb[:], 0.0).then_inc(cleared, 1)

            def copy_turned(c, g):
                p, n, buf = c % 2, BODY // 2 * g + c // 2, c // GROUP % 2
                if c % GROUP == 0:
                    dve.wait_ge(w_done[buf], g + c // BODY)
                dve.wait_ge(t_done[p], n + 1)
                win = ps[:, 2 + p].rearrange("p (k j r) -> p k j r", k=CHUNKS, j=2)[:, :, :, 0:BANDS * WIN]
                win = win.rearrange("p k j (s n) -> p k j s n", s=BANDS)
                to = turned[:, buf, :, c % GROUP].rearrange("p k (s n) -> p k s n", s=BANDS)
                nc.vector.tensor_copy(to[:, :, :, 0:SHIFT], win[:, :, 0, :, 0:SHIFT])
                nc.vector.tensor_copy(to[:, :, :, WIN:COEFS], win[:, :, 1, :, BOTH:WIN])
                nc.vector.tensor_copy(to[:, :, :, SHIFT:WIN], win[:, :, 0, :, SHIFT:WIN]).then_inc(t_half[p], 1)
                dve.wait_ge(t_half[p], n + 1)
                nc.vector.tensor_tensor(to[:, :, :, SHIFT:WIN], to[:, :, :, SHIFT:WIN], win[:, :, 1, :, 0:BOTH],
                                        ALU.add).then_inc(t_copied[p], 1)

            def turn(g):
                for c in range(BODY):
                    copy_turned(c, g)
            turn(0)
            with dve.Fori(1, TURNS) as g:
                turn(g)

            dve.wait_ge(mix_in_loaded, 64)
            dve.wait_ge(cleared, 1)
            def turn(t):
                for b in range(MIX_BUFS):
                    dve.wait_ge(mixed[b], t)
                    for q in range(4):
                        part = slice(32 * q, 32 * q + 32)
                        src = mix_in[part].rearrange("p b (c u) -> p c u b", c=TILES)
                        last = nc.vector.tensor_copy(diag[part, b, :, :, BATCH * q:BATCH * q + BATCH],
                                                     src[:, :, bass.ds(U * MIX_BUFS * t + U * b, U), :])
                    last.then_inc(diag_built[b], 1)
            turn(0)
            with dve.Fori(1, MIX_TURNS) as t:
                turn(t)

            def turn(g):
                for c in range(BODY):
                    slot = c % SLOTS
                    dve.wait_ge(x_loaded[slot], 16 * (2 * TURNS + 2 * g + c // SLOTS + 1))
                    for half in range(2):
                        dve.wait_ge(o_done[half], BODY * g + c + 1)
                        rows = x_sb[:, slot, 2 * half:2 * half + 2]
                        nc.vector.tensor_tensor(rows, ps[:, 2 + 2 * half:4 + 2 * half], rows,
                                                ALU.add).then_inc(added[half], 1)
            turn(0)
            with dve.Fori(1, TURNS) as g:
                turn(g)


def kernel(x, L0_conv_w_yl, L0_conv_w_yh):
    import concourse.bacc as bacc
    from concourse.bass_utils import run_bass_kernel_spmd

    w = np.concatenate([np.asarray(L0_conv_w_yl)[:, :, None], np.asarray(L0_conv_w_yh)], axis=2)
    w = w.reshape(CHANNELS, CHANNELS, BANDS, BANDS, COEFS, 2, HALF)
    w = w.transpose(5, 2, 0, 6, 3, 4, 1).reshape(P, TILES, MIX_CHUNKS, U, CHANNELS)
    w = np.ascontiguousarray(w.transpose(2, 0, 3, 1, 4))
    arrays = {"x": np.ascontiguousarray(x), "weights": w, "consts": constants()}

    nc = bacc.Bacc("TRN2", target_bir_lowering=False, num_devices=1)
    args = [nc.dram_tensor(k, a.shape, F32, kind="ExternalInput").ap() for k, a in arrays.items()]
    out = nc.dram_tensor("out", (BATCH, CHANNELS, SIZE, SIZE), F32, kind="ExternalOutput").ap()
    wavelet_mix_kernel(nc, *args, out)
    r = run_bass_kernel_spmd(nc, [arrays], core_ids=[0])
    return r.results[0]["out"]
```

```python
from contextlib import ExitStack

import numpy as np
import concourse.bass as bass
from concourse import mybir
from concourse.alu_op_type import AluOpType as ALU

F32 = mybir.dt.float32

P = 128
BATCH, CHANNELS, SIZE = 8, 32, 512
IMAGES = BATCH * CHANNELS
CHUNKS = SIZE // P
BANDS, COEFS = 2, 42
ROWS = BANDS * COEFS
HALF = COEFS // 2
HALF_ROWS = BANDS * HALF
WIN = 26
SHIFT = COEFS - WIN
BOTH = WIN - SHIFT

SLOTS = 8
TURNS = IMAGES // SLOTS
TURNS_BATCH = CHANNELS // SLOTS
GROUP = 4

Q = 4
LINES = ROWS // Q
STEPS = -(-LINES // 4)
FULL = LINES // 4
U = 14
PAIRS = ROWS // U // 2
QB = Q * BATCH

LO = np.array([0.11154074335008017, 0.4946238903983854, 0.7511339080215775, 0.3152503517092432,
               -0.22626469396516913, -0.12976686756709563, 0.09750160558707936, 0.02752286553001629,
               -0.031582039318031156, 0.0005538422009938016, 0.004777257511010651, -0.00107730108499558])
TAPS = len(LO)
HI = LO[::-1] * np.where(np.arange(TAPS) % 2, -1.0, 1.0)
LEVELS = 4


def analysis(n, taps):
    out = (n + TAPS - 1) // 2
    pad = (2 * (out - 1) - n + TAPS) // 2
    m = np.zeros((out, n))
    for r in range(out):
        for k in range(TAPS):
            c = 2 * r + k - pad
            c = -1 - c if c < 0 else c
            c = 2 * n - 1 - c if c >= n else c
            m[r, c] += taps[k]
    return m


def synthesis(n, taps):
    m = np.zeros((2 * n + 2 - TAPS, n))
    for s in range(m.shape[0]):
        for r in range(n):
            k = s + TAPS - 2 - 2 * r
            if 0 <= k < TAPS:
                m[s, r] = taps[k]
    return m


def transforms():
    a, s, sizes = np.eye(SIZE), np.eye(SIZE), [SIZE]
    for _ in range(LEVELS - 1):
        a = analysis(sizes[-1], LO) @ a
        s = s @ synthesis(a.shape[0], LO)[:sizes[-1]]
        sizes.append(a.shape[0])
    n = sizes[-1]
    return (np.stack([analysis(n, t) @ a for t in (LO, HI)]),
            np.stack([s @ synthesis(COEFS, t)[:n] for t in (LO, HI)], axis=1))


AH, AW, SW, SH, EYE, NEG = 0, 256, 640, 1152, 1664, 1792
CONSTS = NEG + 32


def constants():
    a, s = transforms()
    c = np.zeros((P, CONSTS))
    for k in range(CHUNKS):
        rows = slice(k * P, (k + 1) * P)
        first = SHIFT * (k // 2)
        c[:, AH + 64 * k:AH + 64 * k + BANDS * WIN] = a[:, first:first + WIN, rows].reshape(BANDS * WIN, P).T
    for j in range(2):
        for n in range(3):
            rows = slice((j + n) * P, (j + n + 1) * P)
            at = AW + 64 * (3 * j + n)
            c[:, at:at + HALF_ROWS] = a[:, HALF * j:HALF * (j + 1), rows].reshape(HALF_ROWS, P).T
    c[:ROWS, SW:SW + SIZE] = s.reshape(SIZE, BANDS, 2, HALF).transpose(2, 1, 3, 0).reshape(ROWS, SIZE)
    c[:ROWS, SH:SH + SIZE] = s.reshape(SIZE, ROWS).T
    c[:, EYE:EYE + P] = np.eye(P)
    c[:, NEG:NEG + 32] = -np.tile(np.eye(32), (4, 1))
    return c.astype(np.float32)


def lines(v):
    return 4 if v < FULL else LINES - 4 * FULL


def wavelet_mix_kernel(nc, x, w_full, w_rest, consts, out):
    x_rows = x.rearrange("b i (c p) w -> (b i) p c w", p=P)
    out_rows = out.rearrange("b i (c p) w -> (b i) p c w", p=P)

    with ExitStack() as ctx:
        def sb(name, shape):
            return ctx.enter_context(nc.sbuf_tensor(name, shape, F32))

        def sem(name):
            return ctx.enter_context(nc.semaphore(name))

        def sems(name, n):
            return [sem(f"{name}{i}") for i in range(n)]

        const = sb("const", [P, CONSTS])
        x_sb = sb("x_sb", [P, SLOTS, CHUNKS, SIZE])
        mix_sb = sb("mix_sb", [P, STEPS, BATCH, 4, ROWS])
        w_sb = sb("w_sb", [P, 2, U, 4, CHANNELS])
        diag = sb("diag", [P, 2, 4, U, QB])
        pick = sb("pick", [P, 2, ROWS])
        spread = sb("spread", [P, 2, SIZE])

        work = sb("work", [P, 2 * CHANNELS * ROWS + STEPS * Q * ROWS])
        along_h = work[:, 0:2 * SIZE].rearrange("p (a w) -> p a w", a=2)
        at = 2 * SIZE
        turned = work[:, at:at + 2 * CHUNKS * GROUP * ROWS].rearrange(
            "p (a k g r) -> p a k g r", a=2, k=CHUNKS, g=GROUP)
        at += 2 * CHUNKS * GROUP * ROWS
        coef = work[:, at:at + CHANNELS * ROWS].rearrange("p (r i) -> p r i", i=CHANNELS)
        delta = work[:, 0:2 * CHANNELS * ROWS].rearrange("p (a r) -> p a r", r=ROWS)
        at = 2 * CHANNELS * ROWS
        stage = work[:, at:at + STEPS * Q * ROWS].rearrange("p (v r) -> p v r", v=STEPS)

        ps = ctx.enter_context(nc.psum_tensor("ps", [P, 8, 512], F32))

        const_loaded = sem("const_loaded")
        cleared = sem("cleared")
        diag_cleared = sem("diag_cleared")
        x_loaded = sems("x_loaded", SLOTS)
        h_done = sems("h_done", SLOTS)
        h_copied = sems("h_copied", 2)
        t_done = sems("t_done", 2)
        t_half = sems("t_half", 2)
        t_copied = sems("t_copied", 2)
        w_done = sems("w_done", 2)
        c_copied = sem("c_copied")
        m_done = sem("m_done")
        m_copied = sem("m_copied")
        w_loaded = sems("w_loaded", 2)
        diag_built = sems("diag_built", 2)
        mixed = sems("mixed", 2)
        mixed_copied = sems("mixed_copied", 2)
        staged = sem("staged")
        d_done = sem("d_done")
        d_copied = sem("d_copied")
        picked = sems("picked", 2)
        s_done = sems("s_done", 2)
        s_copied = sems("s_copied", 2)
        o_done = sems("o_done", 2)
        added = sems("added", 2)
        x_stored = sems("x_stored", SLOTS)

        block = ctx.enter_context(nc.Block())

        @block.gpsimd
        def _(pool):
            nc.gpsimd.memset(mix_sb[:, FULL], 0.0).then_inc(cleared, 1)
            nc.gpsimd.memset(pick[:], 0.0).then_inc(cleared, 1)
            nc.gpsimd.memset(spread[:], 0.0).then_inc(cleared, 1)

        @block.sync
        def _(sp):
            sp.dma_start(const[:], consts).then_inc(const_loaded, 16)

            for c in range(SLOTS):
                sp.dma_start(x_sb[:, c], x_rows[c]).then_inc(x_loaded[c], 16)
            with sp.Fori(1, TURNS) as t:
                for c in range(SLOTS):
                    sp.wait_ge(h_done[c], t)
                    sp.dma_start(x_sb[:, c], x_rows[SLOTS * t + c]).then_inc(x_loaded[c], 16)

            for a in range(2):
                sp.dma_start(w_sb[:, a], w_full[a]).then_inc(w_loaded[a], 16)
            with sp.Fori(1, FULL * PAIRS) as m:
                for a in range(2):
                    sp.wait_ge(mixed[a], m + 1)
                    sp.dma_start(w_sb[:, a], w_full[2 * m + a]).then_inc(w_loaded[a], 16)
            with sp.Fori(0, PAIRS) as m:
                for a in range(2):
                    sp.wait_ge(mixed[a], m + FULL * PAIRS + 1)
                    sp.dma_start(w_sb[:, a, :, 0], w_rest[2 * m + a]).then_inc(w_loaded[a], 16)

            def store(c, t, first):
                sp.wait_ge(added[1], SLOTS * t + c + 2)
                sp.dma_start(out_rows[first + c], x_sb[:, c]).then_inc(x_stored[c], 16)

            def refill(c, t, first):
                sp.wait_ge(x_stored[c], 16 * t)
                sp.dma_start(x_sb[:, c], x_rows[first + c]).then_inc(x_loaded[c], 16)

            for c in range(SLOTS):
                store(c, 0, IMAGES - SLOTS)
                if c >= 2:
                    refill(c - 2, 1, IMAGES - 2 * SLOTS)
            with sp.Fori(1, TURNS - 1) as t:
                first = t * -SLOTS + (IMAGES - SLOTS)
                after = t * -SLOTS + (IMAGES - 2 * SLOTS)
                for c in range(SLOTS):
                    store(c, t, first)
                    if c < 2:
                        refill(c + SLOTS - 2, t, first)
                    else:
                        refill(c - 2, t + 1, after)
            for c in range(SLOTS):
                store(c, TURNS - 1, 0)
                if c < 2:
                    refill(c + SLOTS - 2, TURNS - 1, 0)
            for c in range(SLOTS):
                sp.wait_ge(x_stored[c], 16 * TURNS)

        @block.tensor
        def _(pe):
            for a in range(2):
                pe.sem_inc(mixed[a], 1)
                pe.sem_inc(o_done[a], 1)
            pe.wait_ge(const_loaded, 16)

            def h_stage(c, t):
                p = c % 2
                pe.wait_ge(x_loaded[c], 16 * (t + 1))
                pe.wait_ge(h_copied[p], SLOTS // 2 * t + c // 2)
                for k in (0, 2, 1, 3):
                    j = k // 2
                    last = nc.tensor.matmul(ps[64 * j:64 * j + 64, p], const[:, AH + 64 * k:AH + 64 * k + 64],
                                            x_sb[:, c, k], start=k % 2 == 0, stop=k % 2 == 1)
                last.then_inc(h_done[c], 1)

            def turn_stage(c, t):
                p, n = c % 2, SLOTS // 2 * t + c // 2
                pe.wait_ge(h_copied[p], n + 1)
                pe.wait_ge(t_copied[p], n)
                for k in range(CHUNKS):
                    last = nc.tensor.matmul(ps[:, 2 + p, P * k:P * k + P], along_h[:, p, P * k:P * k + P],
                                            const[:, EYE:EYE + P], start=True, stop=True, is_transpose=True)
                last.then_inc(t_done[p], 1)

            def w_stage(a, n):
                pe.wait_ge(t_copied[1], 2 * (2 * n + a) + 2)
                for k in range(3):
                    for j in range(2):
                        at = AW + 64 * (3 * j + k)
                        last = nc.tensor.matmul(ps[64 * j:64 * j + 64, 4 + a, 0:GROUP * ROWS],
                                                const[:, at:at + 64],
                                                turned[:, a, j + k].rearrange("p g r -> p (g r)"),
                                                start=k == 0, stop=k == 2)
                last.then_inc(w_done[a], 1)

            def channels_stage(v, b):
                if v == 0:
                    pe.wait_ge(c_copied, CHANNELS // GROUP * (b + 1))
                if v >= 2:
                    pe.wait_ge(m_copied, STEPS * b + v - 1)
                for n in range(lines(v)):
                    h = Q * (4 * v + n)
                    last = nc.tensor.matmul(ps[:, 6 + v % 2, P * n:P * n + P],
                                            coef[:, h:h + Q].rearrange("p q i -> p (q i)"),
                                            const[:, EYE:EYE + P], start=True, stop=True, is_transpose=True)
                last.then_inc(m_done, 1)

            def turn1(t, first=False, batch=None):
                for c in range(SLOTS):
                    h_stage(c, t)
                    if c:
                        turn_stage(c - 1, t)
                    elif not first:
                        turn_stage(SLOTS - 1, t - 1)
                    if c == 1 and not first:
                        w_stage(1, t - 1)
                    if c == 5:
                        w_stage(0, t)
                    if batch is not None and 3 <= c <= 5:
                        channels_stage(2 * (c - 3), batch)
                        channels_stage(2 * (c - 3) + 1, batch)

            turn1(0, first=True)
            with pe.Fori(1, TURNS_BATCH) as t:
                turn1(t)
            with pe.Fori(1, BATCH) as b:
                turn1(TURNS_BATCH * b, batch=b - 1)
                with pe.Fori(1, TURNS_BATCH) as r:
                    turn1(TURNS_BATCH * b + r)
            turn_stage(SLOTS - 1, TURNS - 1)
            w_stage(1, TURNS - 1)
            for v in range(STEPS):
                channels_stage(v, BATCH - 1)

            def mix(a, m, tiles):
                pe.wait_ge(diag_built[a], m + 1)
                pe.wait_ge(w_loaded[a], 16 * (m + 1))
                pe.wait_ge(mixed_copied[a], m + 1)
                for n in range(tiles):
                    nc.tensor.matmul(ps[32 * n:32 * n + 32, a, 0:U * QB], const[:, NEG:NEG + 32],
                                     diag[:, a, n].rearrange("p u n -> p (u n)"), start=True, stop=False,
                                     skip_group_check=True)
                for u in range(U):
                    for n in range(tiles):
                        last = nc.tensor.matmul(ps[32 * n:32 * n + 32, a, QB * u:QB * u + QB],
                                                w_sb[:, a, u, n], diag[:, a, n, u],
                                                start=False, stop=u == U - 1, skip_group_check=True)
                last.then_inc(mixed[a], 1)

            with pe.Fori(0, FULL * PAIRS) as m:
                for a in range(2):
                    mix(a, m, 4)
            with pe.Fori(FULL * PAIRS, STEPS * PAIRS) as m:
                for a in range(2):
                    mix(a, m, lines(FULL))
            for a in range(2):
                pe.wait_ge(mixed_copied[a], STEPS * PAIRS + 1)

            def coefs_stage(v, k):
                pe.wait_ge(staged, STEPS * k + v + 1)
                if v >= 2:
                    pe.wait_ge(d_copied, STEPS * k + v - 1)
                for q in range(Q):
                    last = nc.tensor.matmul(ps[0:ROWS, 6 + v % 2, P * q:P * q + P],
                                            stage[:, v, ROWS * q:ROWS * (q + 1)], const[:, EYE:EYE + P],
                                            start=True, stop=True, is_transpose=True)
                last.then_inc(d_done, 1)

            def spread_stage(c, t):
                p, n = c % 2, SLOTS // 2 * t + c // 2
                pe.wait_ge(picked[p], n + 1)
                pe.wait_ge(s_copied[p], n + 1)
                nc.tensor.matmul(ps[0:ROWS, p], pick[:, p], const[:, SW:SW + SIZE],
                                 start=True, stop=True).then_inc(s_done[p], 1)

            def out_stage(c, t):
                p, n = c % 2, SLOTS * t + c
                pe.wait_ge(s_copied[p], SLOTS // 2 * t + c // 2 + 2)
                for half in range(2):
                    pe.wait_ge(added[half], n + 1)
                    for k in (2 * half, 2 * half + 1):
                        last = nc.tensor.matmul(ps[:, 2 + k], const[:, SH + P * k:SH + P * k + P], spread[:, p],
                                                start=True, stop=True)
                    last.then_inc(o_done[half], 1)

            def turn2(t, last=False, batch=None):
                for c in range(SLOTS):
                    if c < SLOTS - 1:
                        spread_stage(c + 1, t)
                    elif not last:
                        spread_stage(0, t + 1)
                    out_stage(c, t)
                    if batch is not None and 1 <= c <= 3:
                        coefs_stage(2 * (c - 1), batch)
                        coefs_stage(2 * (c - 1) + 1, batch)

            for v in range(STEPS):
                coefs_stage(v, 0)
            pe.wait_ge(cleared, 3)
            spread_stage(0, 0)
            with pe.Fori(0, BATCH - 1) as k:
                with pe.Fori(0, TURNS_BATCH - 1) as r:
                    turn2(TURNS_BATCH * k + r)
                turn2(TURNS_BATCH * k + TURNS_BATCH - 1, batch=k + 1)
            with pe.Fori(TURNS - TURNS_BATCH, TURNS - 1) as t:
                turn2(t)
            turn2(TURNS - 1, last=True)

        @block.scalar
        def _(act):
            for a in range(2):
                act.sem_inc(mixed_copied[a], 1)
                act.sem_inc(s_copied[a], 1)
            act.wait_ge(cleared, 3)

            def copy_h(c, t):
                p, n = c % 2, SLOTS // 2 * t + c // 2
                act.wait_ge(h_done[c], t + 1)
                act.wait_ge(t_done[p], n)
                nc.scalar.copy(along_h[:, p], ps[:, p]).then_inc(h_copied[p], 1)

            def copy_c(a, n):
                i = (SLOTS * n + GROUP * a) & (CHANNELS - GROUP)
                act.wait_ge(w_done[a], n + 1)
                nc.scalar.copy(coef[:, :, bass.ds(i, GROUP)],
                               ps[:, 4 + a, 0:GROUP * ROWS].rearrange("p (g r) -> p r g", g=GROUP),
                               ).then_inc(c_copied, 1)

            def copy_m(v, b):
                n = lines(v)
                act.wait_ge(m_done, STEPS * b + v + 1)
                nc.scalar.copy(mix_sb[:, v, b, 0:n].rearrange("p l (j r) -> p l j r", j=2),
                               ps[:, 6 + v % 2, 0:P * n].rearrange("p (l j r) -> p l j r", l=n, j=2)[
                                   :, :, :, 0:HALF_ROWS]).then_inc(m_copied, 1)

            def turn1(t, first=False, batch=None):
                for c in range(SLOTS):
                    copy_h(c, t)
                    if c == 2 and not first:
                        copy_c(1, t - 1)
                    if batch is not None and 3 <= c <= 5:
                        copy_m(2 * (c - 3), batch)
                        copy_m(2 * (c - 3) + 1, batch)
                    if c == 6:
                        copy_c(0, t)

            turn1(0, first=True)
            with act.Fori(1, TURNS_BATCH) as t:
                turn1(t)
            with act.Fori(1, BATCH) as b:
                turn1(TURNS_BATCH * b, batch=b - 1)
                with act.Fori(1, TURNS_BATCH) as r:
                    turn1(TURNS_BATCH * b + r)
            copy_c(1, TURNS - 1)
            for v in range(STEPS):
                copy_m(v, BATCH - 1)

            def copy_mixed(a, m, v, j, n):
                act.wait_ge(mixed[a], m + 2)
                nc.scalar.copy(mix_sb[0:32 * n, v, :, :, bass.ds(2 * U * j + U * a, U)],
                               ps[0:32 * n, a, 0:U * QB].rearrange("p (u q b) -> p b q u", q=Q, b=BATCH),
                               ).then_inc(mixed_copied[a], 1)

            with act.Fori(0, FULL) as v:
                with act.Fori(0, PAIRS) as j:
                    for a in range(2):
                        copy_mixed(a, PAIRS * v + j, v, j, 4)
            with act.Fori(0, PAIRS) as j:
                for a in range(2):
                    copy_mixed(a, FULL * PAIRS + j, FULL, j, lines(FULL))
            for a in range(2):
                act.wait_ge(mixed_copied[a], STEPS * PAIRS + 1)

            def copy_stage(v, k):
                nc.scalar.copy(stage[:, v], mix_sb[:, v, BATCH - 1 - k].rearrange("p q r -> p (q r)"),
                               ).then_inc(staged, 1)

            def copy_delta(v, k):
                n, h = lines(v), 4 * Q * v
                act.wait_ge(d_done, STEPS * k + v + 1)
                to = delta[0:ROWS, bass.ds(CHANNELS * (k & 1), CHANNELS), h:h + Q * n]
                of = ps[0:ROWS, 6 + v % 2].rearrange("p (q l o) -> p o l q", q=Q, l=4)[:, :, 0:n]
                nc.scalar.copy(to.rearrange("p o (l q) -> p o l q", q=Q), of).then_inc(d_copied, 1)

            def pick_image(c, t):
                p, n = c % 2, SLOTS // 2 * t + c // 2
                o = CHANNELS * ((t >> 2) & 1) + CHANNELS - SLOTS - SLOTS * (t & 3) + c
                act.wait_ge(s_done[p], n)
                nc.scalar.copy(pick[0:ROWS, p], delta[0:ROWS, o]).then_inc(picked[p], 1)

            def copy_spread(c, t):
                p, n = c % 2, SLOTS // 2 * t + c // 2
                act.wait_ge(s_done[p], n + 1)
                act.wait_ge(o_done[1], SLOTS * t + c)
                nc.scalar.copy(spread[0:ROWS, p], ps[0:ROWS, p]).then_inc(s_copied[p], 1)

            def turn2(t, last=False, batch=None):
                for c in range(SLOTS):
                    if batch is not None and 2 <= c <= 4:
                        copy_delta(2 * (c - 2), batch)
                        copy_delta(2 * (c - 2) + 1, batch)
                    if c < SLOTS - 2:
                        pick_image(c + 2, t)
                    elif not last:
                        if batch is not None and c == SLOTS - 2:
                            act.wait_ge(d_copied, STEPS * (batch + 1))
                        pick_image(c + 2 - SLOTS, t + 1)
                    if c < SLOTS - 1:
                        copy_spread(c + 1, t)
                    elif not last:
                        copy_spread(0, t + 1)
                    if batch is not None and c <= 2:
                        copy_stage(2 * c, batch)
                        copy_stage(2 * c + 1, batch)

            for v in range(STEPS):
                copy_stage(v, 0)
            for v in range(STEPS):
                copy_delta(v, 0)
            act.wait_ge(d_copied, STEPS)
            pick_image(0, 0)
            pick_image(1, 0)
            copy_spread(0, 0)
            with act.Fori(0, BATCH - 1) as k:
                with act.Fori(0, TURNS_BATCH - 1) as r:
                    turn2(TURNS_BATCH * k + r)
                turn2(TURNS_BATCH * k + TURNS_BATCH - 1, batch=k + 1)
            with act.Fori(TURNS - TURNS_BATCH, TURNS - 1) as t:
                turn2(t)
            turn2(TURNS - 1, last=True)

        @block.vector
        def _(dve):
            for a in range(2):
                dve.sem_inc(added[a], 1)
            nc.vector.memset(diag[:], 0.0).then_inc(diag_cleared, 1)

            def copy_turned(c, t):
                p, n, a = c % 2, SLOTS // 2 * t + c // 2, c // GROUP
                if c % GROUP == 0:
                    dve.wait_ge(w_done[a], t)
                dve.wait_ge(t_done[p], n + 1)
                win = ps[:, 2 + p].rearrange("p (k j r) -> p k j r", k=CHUNKS, j=2)[:, :, :, 0:BANDS * WIN]
                win = win.rearrange("p k j (s n) -> p k j s n", s=BANDS)
                to = turned[:, a, :, c % GROUP].rearrange("p k (s n) -> p k s n", s=BANDS)
                nc.vector.tensor_copy(to[:, :, :, SHIFT:WIN], win[:, :, 0, :, SHIFT:WIN]).then_inc(t_half[p], 1)
                nc.vector.tensor_copy(to[:, :, :, 0:SHIFT], win[:, :, 0, :, 0:SHIFT])
                nc.vector.tensor_copy(to[:, :, :, WIN:COEFS], win[:, :, 1, :, BOTH:WIN])
                dve.wait_ge(t_half[p], n + 1)
                nc.vector.tensor_tensor(to[:, :, :, SHIFT:WIN], to[:, :, :, SHIFT:WIN], win[:, :, 1, :, 0:BOTH],
                                        ALU.add).then_inc(t_copied[p], 1)

            for c in range(SLOTS):
                copy_turned(c, 0)
            with dve.Fori(1, TURNS) as t:
                for c in range(SLOTS):
                    copy_turned(c, t)

            def build_diag(a, m, v, j, n):
                dve.wait_ge(mixed[a], m + 1)
                for q in range(Q):
                    part = slice(32 * q, 32 * q + 32)
                    src = mix_sb[part, v, :, 0:n, bass.ds(2 * U * j + U * a, U)].rearrange("p b l u -> p l u b")
                    last = nc.vector.tensor_copy(diag[part, a, 0:n, :, BATCH * q:BATCH * (q + 1)], src)
                last.then_inc(diag_built[a], 1)

            dve.wait_ge(diag_cleared, 1)
            dve.wait_ge(m_copied, STEPS * BATCH)
            with dve.Fori(0, FULL) as v:
                with dve.Fori(0, PAIRS) as j:
                    for a in range(2):
                        build_diag(a, PAIRS * v + j, v, j, 4)
            with dve.Fori(0, PAIRS) as j:
                for a in range(2):
                    build_diag(a, FULL * PAIRS + j, FULL, j, lines(FULL))

            with dve.Fori(0, TURNS) as t:
                for c in range(SLOTS):
                    dve.wait_ge(x_loaded[c], 16 * (TURNS + t))
                    for half in range(2):
                        dve.wait_ge(o_done[half], SLOTS * t + c + 2)
                        rows = x_sb[:, c, 2 * half:2 * half + 2]
                        nc.vector.tensor_tensor(rows, ps[:, 2 + 2 * half:4 + 2 * half], rows,
                                                ALU.add).then_inc(added[half], 1)


def kernel(x, L0_conv_w_yl, L0_conv_w_yh):
    import concourse.bacc as bacc
    from concourse.bass_utils import run_bass_kernel_spmd

    w = np.concatenate([np.asarray(L0_conv_w_yl)[:, :, None], np.asarray(L0_conv_w_yh)], axis=2)
    w = w.reshape(CHANNELS, CHANNELS, BANDS, BANDS, COEFS, 2, HALF)
    w = w.transpose(0, 1, 3, 4, 5, 2, 6).reshape(CHANNELS, CHANNELS, LINES, Q, 2 * PAIRS, U)
    w = w.transpose(2, 4, 3, 0, 5, 1)
    full = w[:4 * FULL].reshape(FULL, 4, 2 * PAIRS, P, U, CHANNELS).transpose(0, 2, 3, 4, 1, 5)
    full = np.ascontiguousarray(full.reshape(2 * FULL * PAIRS, P, U, 4, CHANNELS))
    rest = np.ascontiguousarray(w[4 * FULL].reshape(2 * PAIRS, P, U, CHANNELS))
    arrays = {"x": np.ascontiguousarray(x), "w_full": full, "w_rest": rest, "consts": constants()}

    nc = bacc.Bacc("TRN2", target_bir_lowering=False, num_devices=1)
    args = [nc.dram_tensor(k, a.shape, F32, kind="ExternalInput").ap() for k, a in arrays.items()]
    out = nc.dram_tensor("out", (BATCH, CHANNELS, SIZE, SIZE), F32, kind="ExternalOutput").ap()
    wavelet_mix_kernel(nc, *args, out)
    r = run_bass_kernel_spmd(nc, [arrays], core_ids=[0])
    return r.results[0]["out"]
```

```python
from contextlib import ExitStack

import numpy as np
import concourse.bass as bass
from concourse import mybir
from concourse.alu_op_type import AluOpType as ALU

F32 = mybir.dt.float32

P = 128
BATCH, CHANNELS, SIZE = 8, 32, 512
IMAGES = BATCH * CHANNELS
CHUNKS = SIZE // P
BANDS, COEFS = 2, 42
ROWS = BANDS * COEFS
HALF = COEFS // 2
HALF_ROWS = BANDS * HALF
WIN = 26
SHIFT = COEFS - WIN
BOTH = WIN - SHIFT

SLOTS = 8
TURNS = IMAGES // SLOTS
TURNS_BATCH = CHANNELS // SLOTS
GROUP = 4

Q = 4
LINES = ROWS // Q
STEPS = -(-LINES // 4)
FULL = LINES // 4
U = 14
PARTS = ROWS // U
WBUFS = 3
QB = Q * BATCH
W_CHUNK = U * 4 * CHANNELS

EARLY = 6

LO = np.array([0.11154074335008017, 0.4946238903983854, 0.7511339080215775, 0.3152503517092432,
               -0.22626469396516913, -0.12976686756709563, 0.09750160558707936, 0.02752286553001629,
               -0.031582039318031156, 0.0005538422009938016, 0.004777257511010651, -0.00107730108499558])
TAPS = len(LO)
HI = LO[::-1] * np.where(np.arange(TAPS) % 2, -1.0, 1.0)
LEVELS = 4


def analysis(n, taps):
    out = (n + TAPS - 1) // 2
    pad = (2 * (out - 1) - n + TAPS) // 2
    m = np.zeros((out, n))
    for r in range(out):
        for k in range(TAPS):
            c = 2 * r + k - pad
            c = -1 - c if c < 0 else c
            c = 2 * n - 1 - c if c >= n else c
            m[r, c] += taps[k]
    return m


def synthesis(n, taps):
    m = np.zeros((2 * n + 2 - TAPS, n))
    for s in range(m.shape[0]):
        for r in range(n):
            k = s + TAPS - 2 - 2 * r
            if 0 <= k < TAPS:
                m[s, r] = taps[k]
    return m


def transforms():
    a, s, sizes = np.eye(SIZE), np.eye(SIZE), [SIZE]
    for _ in range(LEVELS - 1):
        a = analysis(sizes[-1], LO) @ a
        s = s @ synthesis(a.shape[0], LO)[:sizes[-1]]
        sizes.append(a.shape[0])
    n = sizes[-1]
    return (np.stack([analysis(n, t) @ a for t in (LO, HI)]),
            np.stack([s @ synthesis(COEFS, t)[:n] for t in (LO, HI)], axis=1))


AH, AW, SW, SH, EYE, NEG = 0, 256, 640, 1152, 1664, 1792
CONSTS = NEG + 32


def constants():
    a, s = transforms()
    c = np.zeros((P, CONSTS))
    for k in range(CHUNKS):
        rows = slice(k * P, (k + 1) * P)
        first = SHIFT * (k // 2)
        c[:, AH + 64 * k:AH + 64 * k + BANDS * WIN] = a[:, first:first + WIN, rows].reshape(BANDS * WIN, P).T
    for j in range(2):
        for n in range(3):
            rows = slice((j + n) * P, (j + n + 1) * P)
            at = AW + 64 * (3 * j + n)
            c[:, at:at + HALF_ROWS] = a[:, HALF * j:HALF * (j + 1), rows].reshape(HALF_ROWS, P).T
    c[:ROWS, SW:SW + SIZE] = s.reshape(SIZE, BANDS, 2, HALF).transpose(2, 1, 3, 0).reshape(ROWS, SIZE)
    c[:ROWS, SH:SH + SIZE] = s.reshape(SIZE, ROWS).T
    c[:, EYE:EYE + P] = np.eye(P)
    c[:, NEG:NEG + 32] = -np.tile(np.eye(32), (4, 1))
    return c.astype(np.float32)


def lines(v):
    return 4 if v < FULL else LINES - 4 * FULL


def wavelet_mix_kernel(nc, x, w_full, w_rest, consts, out):
    x_rows = x.rearrange("b i (c p) w -> (b i) p c w", p=P)
    out_rows = out.rearrange("b i (c p) w -> (b i) p c w", p=P)

    with ExitStack() as ctx:
        def sb(name, shape):
            return ctx.enter_context(nc.sbuf_tensor(name, shape, F32))

        def sem(name):
            return ctx.enter_context(nc.semaphore(name))

        def sems(name, n):
            return [sem(f"{name}{i}") for i in range(n)]

        const = sb("const", [P, CONSTS])
        x_sb = sb("x_sb", [P, SLOTS, CHUNKS, SIZE])
        mix_sb = sb("mix_sb", [P, STEPS, BATCH, 4, ROWS])
        pick = sb("pick", [P, 2, ROWS])
        spread = sb("spread", [P, 2, SIZE])

        work = sb("work", [P, EARLY * CHUNKS * SIZE])
        along_h = work[:, 0:2 * SIZE].rearrange("p (a w) -> p a w", a=2)
        at = 2 * SIZE
        turned = work[:, at:at + 2 * CHUNKS * GROUP * ROWS].rearrange(
            "p (a k g r) -> p a k g r", a=2, k=CHUNKS, g=GROUP)
        at += 2 * CHUNKS * GROUP * ROWS
        coef = work[:, at:at + CHANNELS * ROWS].rearrange("p (r i) -> p r i", i=CHANNELS)
        used = at + CHANNELS * ROWS
        free = (EARLY * CHUNKS * SIZE - used) // (CHUNKS * SIZE)
        early = work[:, :].rearrange("p (a k w) -> p a k w", a=EARLY, k=CHUNKS)
        early = [early[:, (e - free) % EARLY] for e in range(EARLY)]

        both = sb("both", [P, WBUFS * W_CHUNK + 2 * 4 * U * QB])
        w_sb = both[:, 0:WBUFS * W_CHUNK].rearrange("p (a n) -> p a n", a=WBUFS)
        at = WBUFS * W_CHUNK
        diag = both[:, at:at + 2 * 4 * U * QB].rearrange(
            "p (a l u n) -> p a l u n", a=2, l=4, u=U)
        delta = both[:, 0:2 * CHANNELS * ROWS].rearrange("p (a r) -> p a r", r=ROWS)
        assert 2 * CHANNELS * ROWS <= at
        stage = both[:, at:at + STEPS * Q * ROWS].rearrange("p (v r) -> p v r", v=STEPS)

        ps = ctx.enter_context(nc.psum_tensor("ps", [P, 8, 512], F32))

        const_loaded = sem("const_loaded")
        cleared = sem("cleared")
        diag_cleared = sem("diag_cleared")
        x_loaded = sems("x_loaded", SLOTS)
        h_done = sems("h_done", SLOTS)
        h_copied = sems("h_copied", 2)
        t_done = sems("t_done", 2)
        t_half = sems("t_half", 2)
        t_copied = sems("t_copied", 2)
        w_done = sems("w_done", 2)
        c_copied = sem("c_copied")
        m_done = sem("m_done")
        m_copied = sem("m_copied")
        w_loaded = sems("w_loaded", WBUFS)
        w_ready = sems("w_ready", WBUFS)
        diag_built = sems("diag_built", 2)
        mixed = sems("mixed", 2)
        mixed_copied = sems("mixed_copied", 2)
        first_staged = sem("first_staged")
        staged = sem("staged")
        d_done = sem("d_done")
        d_copied = sem("d_copied")
        picked = sems("picked", 2)
        s_done = sems("s_done", 2)
        s_copied = sems("s_copied", 2)
        o_done = sems("o_done", 2)
        added = sems("added", 2)
        x_stored = sems("x_stored", SLOTS)
        early_loaded = sems("early_loaded", EARLY)
        early_stored = sem("early_stored")

        block = ctx.enter_context(nc.Block())

        @block.gpsimd
        def _(pool):
            nc.gpsimd.memset(mix_sb[:, FULL], 0.0).then_inc(cleared, 1)
            nc.gpsimd.memset(pick[:], 0.0).then_inc(cleared, 1)
            nc.gpsimd.memset(spread[:], 0.0).then_inc(cleared, 1)

        @block.sync
        def _(sp):
            sp.dma_start(const[:], consts).then_inc(const_loaded, 16)

            for c in range(SLOTS):
                sp.dma_start(x_sb[:, c], x_rows[c]).then_inc(x_loaded[c], 16)
            with sp.Fori(1, TURNS) as t:
                for c in range(SLOTS):
                    sp.wait_ge(h_done[c], t)
                    sp.dma_start(x_sb[:, c], x_rows[SLOTS * t + c]).then_inc(x_loaded[c], 16)

            def load_w(c, v, weights):
                sp.dma_start(w_sb[:, c % WBUFS, 0:weights.shape[-1]], weights).then_inc(w_loaded[c % WBUFS], 16)

            def weights_used(c, v):
                sp.wait_ge(mixed[c % 2], PARTS // 2 * v + c // 2 + 2)

            def load_early(e):
                sp.dma_start(early[e], x_rows[IMAGES - 2 * SLOTS + e]).then_inc(early_loaded[e], 16)

            for c in range(WBUFS):
                load_w(c, 0, w_full[c])
            for e in range(free):
                load_early(e)
            for c in range(WBUFS, PARTS):
                weights_used(c - WBUFS, 0)
                load_w(c, 0, w_full[c])
                sp.wait_ge(m_done, STEPS * BATCH)
                load_early(free + c - WBUFS)
            with sp.Fori(1, FULL) as v:
                for c in range(PARTS):
                    if c < WBUFS:
                        weights_used(c + PARTS - WBUFS, v - 1)
                    else:
                        weights_used(c - WBUFS, v)
                    load_w(c, v, w_full[PARTS * v + c])
            for e in range(free + WBUFS, EARLY):
                load_early(e)
            for c in range(PARTS):
                if c < WBUFS:
                    weights_used(c + PARTS - WBUFS, FULL - 1)
                else:
                    weights_used(c - WBUFS, FULL)
                load_w(c, FULL, w_rest[c])

            def store(c, t, first):
                sp.wait_ge(added[1], SLOTS * t + c + 2)
                sp.dma_start(out_rows[first + c], x_sb[:, c]).then_inc(x_stored[c], 16)

            def refill(c, t, first):
                sp.wait_ge(x_stored[c], 16 * (t - (c < EARLY)))
                sp.dma_start(x_sb[:, c], x_rows[first + c]).then_inc(x_loaded[c], 16)

            for c in range(SLOTS):
                store(c, 0, IMAGES - SLOTS)
                if 2 <= c < 2 + EARLY:
                    refill(c - 2, 2, IMAGES - 3 * SLOTS)
                elif c >= 2:
                    refill(c - 2, 1, IMAGES - 2 * SLOTS)
            for c in range(SLOTS):
                if c < EARLY:
                    sp.wait_ge(added[1], SLOTS + c + 2)
                    sp.dma_start(out_rows[IMAGES - 2 * SLOTS + c], early[c]).then_inc(early_stored, 16)
                else:
                    store(c, 1, IMAGES - 2 * SLOTS)
                if c < 2:
                    refill(c + SLOTS - 2, 1, IMAGES - 2 * SLOTS)
                elif c >= 2 + EARLY:
                    refill(c - 2, 2, IMAGES - 3 * SLOTS)
            with sp.Fori(2, TURNS - 1) as t:
                first = t * -SLOTS + (IMAGES - SLOTS)
                after = t * -SLOTS + (IMAGES - 2 * SLOTS)
                for c in range(SLOTS):
                    store(c, t, first)
                    if c < 2:
                        refill(c + SLOTS - 2, t, first)
                    else:
                        refill(c - 2, t + 1, after)
            for c in range(SLOTS):
                store(c, TURNS - 1, 0)
                if c < 2:
                    refill(c + SLOTS - 2, TURNS - 1, 0)
            sp.wait_ge(early_stored, 16 * EARLY)
            for c in range(SLOTS):
                sp.wait_ge(x_stored[c], 16 * (TURNS - (c < EARLY)))

        @block.tensor
        def _(pe):
            for a in range(2):
                pe.sem_inc(mixed[a], 1)
                pe.sem_inc(o_done[a], 1)
            pe.wait_ge(const_loaded, 16)

            def h_stage(c, t):
                p = c % 2
                pe.wait_ge(x_loaded[c], 16 * (t + 1))
                pe.wait_ge(h_copied[p], SLOTS // 2 * t + c // 2)
                for k in (0, 2, 1, 3):
                    j = k // 2
                    last = nc.tensor.matmul(ps[64 * j:64 * j + 64, p], const[:, AH + 64 * k:AH + 64 * k + 64],
                                            x_sb[:, c, k], start=k % 2 == 0, stop=k % 2 == 1)
                last.then_inc(h_done[c], 1)

            def turn_stage(c, t):
                p, n = c % 2, SLOTS // 2 * t + c // 2
                pe.wait_ge(h_copied[p], n + 1)
                pe.wait_ge(t_copied[p], n)
                for k in range(CHUNKS):
                    last = nc.tensor.matmul(ps[:, 2 + p, P * k:P * k + P], along_h[:, p, P * k:P * k + P],
                                            const[:, EYE:EYE + P], start=True, stop=True, is_transpose=True)
                last.then_inc(t_done[p], 1)

            def w_stage(a, n):
                pe.wait_ge(t_copied[1], 2 * (2 * n + a) + 2)
                for k in range(3):
                    for j in range(2):
                        at = AW + 64 * (3 * j + k)
                        last = nc.tensor.matmul(ps[64 * j:64 * j + 64, 4 + a, 0:GROUP * ROWS],
                                                const[:, at:at + 64],
                                                turned[:, a, j + k].rearrange("p g r -> p (g r)"),
                                                start=k == 0, stop=k == 2)
                last.then_inc(w_done[a], 1)

            def channels_stage(v, b):
                if v == 0:
                    pe.wait_ge(c_copied, CHANNELS // GROUP * (b + 1))
                if v >= 2:
                    pe.wait_ge(m_copied, STEPS * b + v - 1)
                for n in range(lines(v)):
                    h = Q * (4 * v + n)
                    last = nc.tensor.matmul(ps[:, 6 + v % 2, P * n:P * n + P],
                                            coef[:, h:h + Q].rearrange("p q i -> p (q i)"),
                                            const[:, EYE:EYE + P], start=True, stop=True, is_transpose=True)
                last.then_inc(m_done, 1)

            def turn1(t, first=False, batch=None):
                for c in range(SLOTS):
                    h_stage(c, t)
                    if c:
                        turn_stage(c - 1, t)
                    elif not first:
                        turn_stage(SLOTS - 1, t - 1)
                    if c == 1 and not first:
                        w_stage(1, t - 1)
                    if c == 5:
                        w_stage(0, t)
                    if batch is not None and 3 <= c <= 5:
                        channels_stage(2 * (c - 3), batch)
                        channels_stage(2 * (c - 3) + 1, batch)

            turn1(0, first=True)
            with pe.Fori(1, TURNS_BATCH) as t:
                turn1(t)
            with pe.Fori(1, BATCH) as b:
                turn1(TURNS_BATCH * b, batch=b - 1)
                with pe.Fori(1, TURNS_BATCH) as r:
                    turn1(TURNS_BATCH * b + r)
            turn_stage(SLOTS - 1, TURNS - 1)
            w_stage(1, TURNS - 1)
            for v in range(STEPS):
                channels_stage(v, BATCH - 1)

            def mix(c, v, n):
                a, wb = c % 2, c % WBUFS
                w = w_sb[:, wb, 0:U * n * CHANNELS].rearrange("p (u l o) -> p u l o", u=U, l=n)
                pe.wait_ge(diag_built[a], PARTS // 2 * v + c // 2 + 1)
                pe.wait_ge(w_ready[wb], PARTS // WBUFS * v + c // WBUFS + 1)
                pe.wait_ge(mixed_copied[a], PARTS // 2 * v + c // 2 + 1)
                for u in range(U):
                    for l in range(n):
                        last = nc.tensor.matmul(ps[32 * l:32 * l + 32, a, QB * u:QB * u + QB],
                                                w[:, u, l], diag[:, a, l, u], start=True, stop=True)
                last.then_inc(mixed[a], 1)

            with pe.Fori(0, FULL) as v:
                for c in range(PARTS):
                    mix(c, v, 4)
            for c in range(PARTS):
                mix(c, FULL, lines(FULL))
            for a in range(2):
                pe.wait_ge(mixed_copied[a], STEPS * PARTS // 2 + 1)

            def coefs_stage(v, k, first=False):
                if first:
                    pe.wait_ge(first_staged, v + 1)
                else:
                    pe.wait_ge(staged, STEPS * (k - 1) + v + 1)
                if v >= 2:
                    pe.wait_ge(d_copied, STEPS * k + v - 1)
                for q in range(Q):
                    last = nc.tensor.matmul(ps[0:ROWS, 6 + v % 2, P * q:P * q + P],
                                            stage[:, v, ROWS * q:ROWS * (q + 1)], const[:, EYE:EYE + P],
                                            start=True, stop=True, is_transpose=True)
                last.then_inc(d_done, 1)

            def spread_stage(c, t):
                p, n = c % 2, SLOTS // 2 * t + c // 2
                pe.wait_ge(picked[p], n + 1)
                pe.wait_ge(s_copied[p], n + 1)
                nc.tensor.matmul(ps[0:ROWS, p], pick[:, p], const[:, SW:SW + SIZE],
                                 start=True, stop=True).then_inc(s_done[p], 1)

            def out_stage(c, t):
                p, n = c % 2, SLOTS * t + c
                pe.wait_ge(s_copied[p], SLOTS // 2 * t + c // 2 + 2)
                for half in range(2):
                    pe.wait_ge(added[half], n + 1)
                    for k in (2 * half, 2 * half + 1):
                        last = nc.tensor.matmul(ps[:, 2 + k], const[:, SH + P * k:SH + P * k + P], spread[:, p],
                                                start=True, stop=True)
                    last.then_inc(o_done[half], 1)

            def turn2(t, last=False, batch=None):
                for c in range(SLOTS):
                    if c < SLOTS - 1:
                        spread_stage(c + 1, t)
                    elif not last:
                        spread_stage(0, t + 1)
                    out_stage(c, t)
                    if batch is not None and 1 <= c <= 3:
                        coefs_stage(2 * (c - 1), batch)
                        coefs_stage(2 * (c - 1) + 1, batch)

            for v in range(STEPS):
                coefs_stage(v, 0, first=True)
            pe.wait_ge(cleared, 3)
            spread_stage(0, 0)
            with pe.Fori(0, BATCH - 1) as k:
                with pe.Fori(0, TURNS_BATCH - 1) as r:
                    turn2(TURNS_BATCH * k + r)
                turn2(TURNS_BATCH * k + TURNS_BATCH - 1, batch=k + 1)
            with pe.Fori(TURNS - TURNS_BATCH, TURNS - 1) as t:
                turn2(t)
            turn2(TURNS - 1, last=True)

        @block.scalar
        def _(act):
            for a in range(2):
                act.sem_inc(mixed_copied[a], 1)
                act.sem_inc(s_copied[a], 1)
            act.wait_ge(cleared, 3)

            def copy_h(c, t):
                p, n = c % 2, SLOTS // 2 * t + c // 2
                act.wait_ge(h_done[c], t + 1)
                act.wait_ge(t_done[p], n)
                nc.scalar.copy(along_h[:, p], ps[:, p]).then_inc(h_copied[p], 1)

            def copy_c(a, n):
                i = (SLOTS * n + GROUP * a) & (CHANNELS - GROUP)
                act.wait_ge(w_done[a], n + 1)
                nc.scalar.copy(coef[:, :, bass.ds(i, GROUP)],
                               ps[:, 4 + a, 0:GROUP * ROWS].rearrange("p (g r) -> p r g", g=GROUP),
                               ).then_inc(c_copied, 1)

            def copy_m(v, b):
                n = lines(v)
                act.wait_ge(m_done, STEPS * b + v + 1)
                nc.scalar.copy(mix_sb[:, v, b, 0:n].rearrange("p l (j r) -> p l j r", j=2),
                               ps[:, 6 + v % 2, 0:P * n].rearrange("p (l j r) -> p l j r", l=n, j=2)[
                                   :, :, :, 0:HALF_ROWS]).then_inc(m_copied, 1)

            def turn1(t, first=False, batch=None):
                for c in range(SLOTS):
                    copy_h(c, t)
                    if c == 2 and not first:
                        copy_c(1, t - 1)
                    if batch is not None and 3 <= c <= 5:
                        copy_m(2 * (c - 3), batch)
                        copy_m(2 * (c - 3) + 1, batch)
                    if c == 6:
                        copy_c(0, t)

            turn1(0, first=True)
            with act.Fori(1, TURNS_BATCH) as t:
                turn1(t)
            with act.Fori(1, BATCH) as b:
                turn1(TURNS_BATCH * b, batch=b - 1)
                with act.Fori(1, TURNS_BATCH) as r:
                    turn1(TURNS_BATCH * b + r)
            copy_c(1, TURNS - 1)
            for v in range(STEPS):
                copy_m(v, BATCH - 1)

            def copy_mixed(c, v, n):
                a = c % 2
                act.wait_ge(mixed[a], PARTS // 2 * v + c // 2 + 2)
                nc.scalar.copy(mix_sb[0:32 * n, v, :, :, U * c:U * c + U],
                               ps[0:32 * n, a, 0:U * QB].rearrange("p (u q b) -> p b q u", q=Q, b=BATCH),
                               ).then_inc(mixed_copied[a], 1)

            with act.Fori(0, FULL) as v:
                for c in range(PARTS):
                    copy_mixed(c, v, 4)
            for c in range(PARTS):
                copy_mixed(c, FULL, lines(FULL))

            def copy_stage(v, k):
                nc.scalar.copy(stage[:, v], mix_sb[:, v, BATCH - 1 - k].rearrange("p q r -> p (q r)"),
                               ).then_inc(staged, 1)

            def copy_delta(v, k):
                n, h = lines(v), 4 * Q * v
                act.wait_ge(d_done, STEPS * k + v + 1)
                to = delta[0:ROWS, bass.ds(CHANNELS * (k & 1), CHANNELS), h:h + Q * n]
                of = ps[0:ROWS, 6 + v % 2].rearrange("p (q l o) -> p o l q", q=Q, l=4)[:, :, 0:n]
                nc.scalar.copy(to.rearrange("p o (l q) -> p o l q", q=Q), of).then_inc(d_copied, 1)

            def pick_image(c, t):
                p, n = c % 2, SLOTS // 2 * t + c // 2
                o = CHANNELS * ((t >> 2) & 1) + CHANNELS - SLOTS - SLOTS * (t & 3) + c
                act.wait_ge(s_done[p], n)
                nc.scalar.copy(pick[0:ROWS, p], delta[0:ROWS, o]).then_inc(picked[p], 1)

            def copy_spread(c, t):
                p, n = c % 2, SLOTS // 2 * t + c // 2
                act.wait_ge(s_done[p], n + 1)
                act.wait_ge(o_done[1], SLOTS * t + c)
                nc.scalar.copy(spread[0:ROWS, p], ps[0:ROWS, p]).then_inc(s_copied[p], 1)

            def turn2(t, last=False, batch=None):
                for c in range(SLOTS):
                    if batch is not None and 2 <= c <= 4:
                        copy_delta(2 * (c - 2), batch)
                        copy_delta(2 * (c - 2) + 1, batch)
                    if c < SLOTS - 2:
                        pick_image(c + 2, t)
                    elif not last:
                        if batch is not None and c == SLOTS - 2:
                            act.wait_ge(d_copied, STEPS * (batch + 1))
                        pick_image(c + 2 - SLOTS, t + 1)
                    if c < SLOTS - 1:
                        copy_spread(c + 1, t)
                    elif not last:
                        copy_spread(0, t + 1)
                    if batch is not None and c <= 2:
                        copy_stage(2 * c, batch)
                        copy_stage(2 * c + 1, batch)

            for v in range(STEPS):
                copy_delta(v, 0)
            act.wait_ge(d_copied, STEPS)
            pick_image(0, 0)
            pick_image(1, 0)
            copy_spread(0, 0)
            with act.Fori(0, BATCH - 1) as k:
                with act.Fori(0, TURNS_BATCH - 1) as r:
                    turn2(TURNS_BATCH * k + r)
                turn2(TURNS_BATCH * k + TURNS_BATCH - 1, batch=k + 1)
            with act.Fori(TURNS - TURNS_BATCH, TURNS - 1) as t:
                turn2(t)
            turn2(TURNS - 1, last=True)

        @block.vector
        def _(dve):
            for a in range(2):
                dve.sem_inc(added[a], 1)
            nc.vector.memset(diag[:], 0.0).then_inc(diag_cleared, 1)

            def copy_turned(c, t):
                p, n, a = c % 2, SLOTS // 2 * t + c // 2, c // GROUP
                if c % GROUP == 0:
                    dve.wait_ge(w_done[a], t)
                dve.wait_ge(t_done[p], n + 1)
                win = ps[:, 2 + p].rearrange("p (k j r) -> p k j r", k=CHUNKS, j=2)[:, :, :, 0:BANDS * WIN]
                win = win.rearrange("p k j (s n) -> p k j s n", s=BANDS)
                to = turned[:, a, :, c % GROUP].rearrange("p k (s n) -> p k s n", s=BANDS)
                nc.vector.tensor_copy(to[:, :, :, SHIFT:WIN], win[:, :, 0, :, SHIFT:WIN]).then_inc(t_half[p], 1)
                nc.vector.tensor_copy(to[:, :, :, 0:SHIFT], win[:, :, 0, :, 0:SHIFT])
                nc.vector.tensor_copy(to[:, :, :, WIN:COEFS], win[:, :, 1, :, BOTH:WIN])
                dve.wait_ge(t_half[p], n + 1)
                nc.vector.tensor_tensor(to[:, :, :, SHIFT:WIN], to[:, :, :, SHIFT:WIN], win[:, :, 1, :, 0:BOTH],
                                        ALU.add).then_inc(t_copied[p], 1)

            for c in range(SLOTS):
                copy_turned(c, 0)
            with dve.Fori(1, TURNS) as t:
                for c in range(SLOTS):
                    copy_turned(c, t)

            def build(c, v, n):
                a, wb = c % 2, c % WBUFS
                dve.wait_ge(mixed[a], PARTS // 2 * v + c // 2 + 1)
                for q in range(Q):
                    part = slice(32 * q, 32 * q + 32)
                    src = mix_sb[part, v, :, 0:n, U * c:U * c + U].rearrange("p b l u -> p l u b")
                    last = nc.vector.tensor_copy(diag[part, a, 0:n, :, BATCH * q:BATCH * (q + 1)], src)
                last.then_inc(diag_built[a], 1)
                dve.wait_ge(w_loaded[wb], 16 * (PARTS // WBUFS * v + c // WBUFS + 1))
                w = w_sb[:, wb, 0:U * n * CHANNELS].rearrange("p (k o) -> p k o", o=CHANNELS)
                minus_eye = const[:, NEG:NEG + CHANNELS].rearrange("p (k o) -> p k o", k=1)
                nc.vector.tensor_tensor(w, w, minus_eye.to_broadcast([P, U * n, CHANNELS]),
                                        ALU.add).then_inc(w_ready[wb], 1)

            dve.wait_ge(diag_cleared, 1)
            dve.wait_ge(const_loaded, 16)
            with dve.Fori(0, FULL) as v:
                dve.wait_ge(m_copied, STEPS * (BATCH - 1) + v + 1)
                for c in range(PARTS):
                    build(c, v, 4)
            dve.wait_ge(m_copied, STEPS * BATCH)
            for c in range(PARTS):
                build(c, FULL, lines(FULL))

            for a in range(2):
                dve.wait_ge(mixed_copied[a], STEPS * PARTS // 2 + 1)
            for v in range(STEPS):
                nc.vector.tensor_copy(stage[:, v], mix_sb[:, v, BATCH - 1].rearrange("p q r -> p (q r)"),
                                      ).then_inc(first_staged, 1)

            def add(c, t, rows):
                for half in range(2):
                    dve.wait_ge(o_done[half], SLOTS * t + c + 2)
                    part = rows[:, 2 * half:2 * half + 2]
                    nc.vector.tensor_tensor(part, ps[:, 2 + 2 * half:4 + 2 * half], part,
                                            ALU.add).then_inc(added[half], 1)

            for c in range(SLOTS):
                add(c, 0, x_sb[:, c])
            for c in range(SLOTS):
                if c < EARLY:
                    dve.wait_ge(early_loaded[c], 16)
                    add(c, 1, early[c])
                else:
                    dve.wait_ge(x_loaded[c], 16 * (TURNS + 1))
                    add(c, 1, x_sb[:, c])
            with dve.Fori(2, TURNS) as t:
                for c in range(SLOTS):
                    dve.wait_ge(x_loaded[c], 16 * (TURNS + t - (c < EARLY)))
                    add(c, t, x_sb[:, c])


def kernel(x, L0_conv_w_yl, L0_conv_w_yh):
    import concourse.bacc as bacc
    from concourse.bass_utils import run_bass_kernel_spmd

    w = np.concatenate([np.asarray(L0_conv_w_yl)[:, :, None], np.asarray(L0_conv_w_yh)], axis=2)
    w = w.reshape(CHANNELS, CHANNELS, BANDS, BANDS, COEFS, 2, HALF)
    w = w.transpose(0, 1, 3, 4, 5, 2, 6).reshape(CHANNELS, CHANNELS, LINES, Q, PARTS, U)
    w = w.transpose(2, 4, 3, 0, 5, 1)
    full = w[:4 * FULL].reshape(FULL, 4, PARTS, P, U, CHANNELS).transpose(0, 2, 3, 4, 1, 5)
    full = np.ascontiguousarray(full.reshape(FULL * PARTS, P, U * 4 * CHANNELS))
    rest = np.ascontiguousarray(w[4 * FULL].reshape(PARTS, P, U * CHANNELS))
    arrays = {"x": np.ascontiguousarray(x), "w_full": full, "w_rest": rest, "consts": constants()}

    nc = bacc.Bacc("TRN2", target_bir_lowering=False, num_devices=1,
                   dynamic_dma_scratch_size=1024)
    args = [nc.dram_tensor(k, a.shape, F32, kind="ExternalInput").ap() for k, a in arrays.items()]
    out = nc.dram_tensor("out", (BATCH, CHANNELS, SIZE, SIZE), F32, kind="ExternalOutput").ap()
    wavelet_mix_kernel(nc, *args, out)
    r = run_bass_kernel_spmd(nc, [arrays], core_ids=[0])
    return r.results[0]["out"]
```
